# Optimizing a Trainium2 kernel written in Bass

```python
import numpy as np
import jax
import jax.numpy as jnp

def _softmax(x, axis=-1):
    return jax.nn.softmax(x, axis=axis)

def _gelu(x):
    return jax.nn.gelu(x, approximate=True)

def _silu(x):
    return jax.nn.silu(x)

def _sigmoid(x):
    return jax.nn.sigmoid(x)

def _layernorm(x, axis=-1, eps=1e-05):
    m = jnp.mean(x, axis=axis, keepdims=True)
    v = jnp.var(x, axis=axis, keepdims=True)
    return (x - m) / jnp.sqrt(v + eps)

def _scatter_add(tgt, idx, src, axis=0):
    return tgt.at[idx].add(src)

def _segment_sum(src, seg, n):
    return jax.ops.segment_sum(src, seg, n)
kernel_name = 'mk_rec_standalone_d1_rec_r8_43b0fc'

def setup_inputs(seed: int=0):
    np.random.seed(seed)
    _w = jnp.asarray

    def _rec_inputs():
        import jax
        import jax.numpy as jnp
        _rk = jax.random.key(seed)
        r_dense = -0.00338568 + 1.0005 * jax.random.normal(jax.random.fold_in(_rk, 1), (2048, 13), jnp.float32)
        r_sparse_idx = jnp.stack([jax.random.randint(jax.random.fold_in(jax.random.fold_in(_rk, 2), 0), (2048,), 2, 12500, jnp.int32), jax.random.randint(jax.random.fold_in(jax.random.fold_in(_rk, 2), 1), (2048,), 1, 99999, jnp.int32), jax.random.randint(jax.random.fold_in(jax.random.fold_in(_rk, 2), 2), (2048,), 0, 12500, jnp.int32), jax.random.randint(jax.random.fold_in(jax.random.fold_in(_rk, 2), 3), (2048,), 5, 12500, jnp.int32), jax.random.randint(jax.random.fold_in(jax.random.fold_in(_rk, 2), 4), (2048,), 20, 99993, jnp.int32), jax.random.randint(jax.random.fold_in(jax.random.fold_in(_rk, 2), 5), (2048,), 0, 99993, jnp.int32), jax.random.randint(jax.random.fold_in(jax.random.fold_in(_rk, 2), 6), (2048,), 2, 99999, jnp.int32), jax.random.randint(jax.random.fold_in(jax.random.fold_in(_rk, 2), 7), (2048,), 2, 99995, jnp.int32), jax.random.randint(jax.random.fold_in(jax.random.fold_in(_rk, 2), 8), (2048,), 0, 99999, jnp.int32), jax.random.randint(jax.random.fold_in(jax.random.fold_in(_rk, 2), 9), (2048,), 2, 99986, jnp.int32), jax.random.randint(jax.random.fold_in(jax.random.fold_in(_rk, 2), 10), (2048,), 4, 99999, jnp.int32), jax.random.randint(jax.random.fold_in(jax.random.fold_in(_rk, 2), 11), (2048,), 15, 99999, jnp.int32), jax.random.randint(jax.random.fold_in(jax.random.fold_in(_rk, 2), 12), (2048,), 0, 99989, jnp.int32), jax.random.randint(jax.random.fold_in(jax.random.fold_in(_rk, 2), 13), (2048,), 5, 99990, jnp.int32), jax.random.randint(jax.random.fold_in(jax.random.fold_in(_rk, 2), 14), (2048,), 2, 99996, jnp.int32), jax.random.randint(jax.random.fold_in(jax.random.fold_in(_rk, 2), 15), (2048,), 3, 99994, jnp.int32), jax.random.randint(jax.random.fold_in(jax.random.fold_in(_rk, 2), 16), (2048,), 0, 99998, jnp.int32), jax.random.randint(jax.random.fold_in(jax.random.fold_in(_rk, 2), 17), (2048,), 13, 99998, jnp.int32), jax.random.randint(jax.random.fold_in(jax.random.fold_in(_rk, 2), 18), (2048,), 10, 12498, jnp.int32), jax.random.randint(jax.random.fold_in(jax.random.fold_in(_rk, 2), 19), (2048,), 0, 99999, jnp.int32), jax.random.randint(jax.random.fold_in(jax.random.fold_in(_rk, 2), 20), (2048,), 0, 99995, jnp.int32), jax.random.randint(jax.random.fold_in(jax.random.fold_in(_rk, 2), 21), (2048,), 1, 99998, jnp.int32), jax.random.randint(jax.random.fold_in(jax.random.fold_in(_rk, 2), 22), (2048,), 1, 99997, jnp.int32), jax.random.randint(jax.random.fold_in(jax.random.fold_in(_rk, 2), 23), (2048,), 2, 99989, jnp.int32), jax.random.randint(jax.random.fold_in(jax.random.fold_in(_rk, 2), 24), (2048,), 6, 12500, jnp.int32), jax.random.randint(jax.random.fold_in(jax.random.fold_in(_rk, 2), 25), (2048,), 2, 99995, jnp.int32)], axis=1)
        return (r_dense, r_sparse_idx)
    r_dense, r_sparse_idx = _rec_inputs()

    def _L0_rec_setup():
        import jax, jax.numpy as jnp
        import numpy as np
        B, F, V, D, ND = (2048, 26, 12500, 64, 13)
        H1, H2, H3 = (1024, 512, 256)
        key = jax.random.key(seed)
        ks = jax.random.split(key, 12)
        s = 0.02
        return {'dense': jax.random.normal(ks[0], (B, ND), jnp.float32), 'sparse_idx': jax.random.randint(ks[1], (B, F), 0, V), 'bias': jnp.zeros((1, 1), jnp.float32), 'emb_tables': jax.random.normal(ks[2], (F, V, D), jnp.float32) * s, 'lin_tables': jax.random.normal(ks[3], (F, V), jnp.float32) * s, 'Wd': jax.random.normal(ks[4], (ND, D), jnp.float32) * s, 'Wld': jax.random.normal(ks[5], (ND, 1), jnp.float32) * s, 'bld': jnp.zeros((1,), jnp.float32), 'W1': jax.random.normal(ks[6], ((F + 1) * D, H1), jnp.float32) * s, 'W2': jax.random.normal(ks[7], (H1, H2), jnp.float32) * s, 'W3': jax.random.normal(ks[8], (H2, H3), jnp.float32) * s, 'Wout': jax.random.normal(ks[9], (H3, 1), jnp.float32) * s}
    _L0_rec_all = _L0_rec_setup()
    _L0_rec_in = {k: v for k, v in _L0_rec_all.items() if k in ('bias', 'emb_tables', 'lin_tables', 'Wd', 'Wld', 'bld', 'W1', 'W2', 'W3', 'Wout')}
    del _L0_rec_all
    return {'r_dense': r_dense, 'r_sparse_idx': r_sparse_idx, 'L0_rec_bias': _L0_rec_in['bias'], 'L0_rec_emb_tables': _L0_rec_in['emb_tables'], 'L0_rec_lin_tables': _L0_rec_in['lin_tables'], 'L0_rec_Wd': _L0_rec_in['Wd'], 'L0_rec_Wld': _L0_rec_in['Wld'], 'L0_rec_bld': _L0_rec_in['bld'], 'L0_rec_W1': _L0_rec_in['W1'], 'L0_rec_W2': _L0_rec_in['W2'], 'L0_rec_W3': _L0_rec_in['W3'], 'L0_rec_Wout': _L0_rec_in['Wout']}

def reference(r_dense, r_sparse_idx, L0_rec_bias, L0_rec_emb_tables, L0_rec_lin_tables, L0_rec_Wd, L0_rec_Wld, L0_rec_bld, L0_rec_W1, L0_rec_W2, L0_rec_W3, L0_rec_Wout):
    import jax
    import jax.numpy as jnp

    def _L0_rec_ref(dense, sparse_idx, bias, emb_tables, lin_tables, Wd, Wld, bld, W1, W2, W3, Wout):
        import jax, jax.numpy as jnp
        import numpy as np
        B, F, V, D, ND = (2048, 26, 12500, 64, 13)
        H1, H2, H3 = (1024, 512, 256)
        feat = jnp.arange(F)[None, :]
        sparse_emb = emb_tables[feat, sparse_idx]
        dense_emb = dense @ Wd
        emb = jnp.concatenate([dense_emb[:, None, :], sparse_emb], axis=1)
        first = dense @ Wld + bld + lin_tables[feat, sparse_idx].sum(axis=1, keepdims=True)
        sum_e = emb.sum(axis=1)
        second = 0.5 * (sum_e * sum_e - (emb * emb).sum(axis=1)).sum(axis=1, keepdims=True)
        h = emb.reshape(emb.shape[0], -1)
        h = jax.nn.relu(h @ W1)
        h = jax.nn.relu(h @ W2)
        h = jax.nn.relu(h @ W3)
        deep = h @ Wout
        return bias + first + second + deep
    y = _L0_rec_ref(r_dense, r_sparse_idx, L0_rec_bias, L0_rec_emb_tables, L0_rec_lin_tables, L0_rec_Wd, L0_rec_Wld, L0_rec_bld, L0_rec_W1, L0_rec_W2, L0_rec_W3, L0_rec_Wout)
    return y

_drawn_inputs = setup_inputs


def setup_inputs(seed=0):
    import zlib

    import numpy as np

    out = dict(_drawn_inputs(seed))
    spreads = {}
    factors = {'L0_rec_W1': 8.0,
     'L0_rec_W2': 8.0,
     'L0_rec_W3': 8.0,
     'L0_rec_Wout': 8.0,
     'L0_rec_Wld': 3.09}
    for name, (base, spread) in spreads.items():
        noise = np.random.default_rng([zlib.crc32(name.encode()), seed]).standard_normal(out[name].shape)
        drawn = base * np.exp(spread * noise) if base else spread * noise
        out[name] = jnp.asarray(drawn.astype(out[name].dtype))
    for name, factor in factors.items():
        out[name] = (out[name] * factor).astype(out[name].dtype)
    return out
```

```python
from contextlib import ExitStack

import concourse.bass as bass
from concourse import mybir

F32 = mybir.dt.float32
F32R = mybir.dt.float32r
I32 = mybir.dt.int32
ALU = mybir.AluOpType
ACT = mybir.ActivationFunctionType
AX = mybir.AxisListType

P = 128
BATCH, FEATURES, VOCAB, DIM = 2048, 26, 12500, 64
H1, H2, H3 = 1024, 512, 256
ROW = DIM + 1
AUG = 13 + 2
TILES = BATCH // P
GT = 2
N = GT * P
GROUPS = TILES // GT
CHUNKS = FEATURES * DIM // P
FPC = P // DIM
PAIR = FPC * ROW
EMB = slice(1, 1 + P)
M1, M2, M3 = H1 // P, H2 // P, H3 // P
UNIT = 1024
BLOCKS = [(0, 3), (3, 6), (6, 9), (9, 13)]
NB = len(BLOCKS)
SQUARES = GT * (NB + 2)
STEPS = CHUNKS + 1
ROWS_CUT = 7
UNITS = 1 + CHUNKS + H1 * H2 // P // UNIT + H2 * H3 // P // UNIT
BANK = 512


def deepfm(nc, table, idx, dense_t, dense_w, w1, w2, w3, w_out, out):
    ctx = ExitStack()
    with ctx:
        def sb(name, shape, dt):
            return ctx.enter_context(nc.sbuf_tensor(name, shape, dt))

        def sem(name):
            return ctx.enter_context(nc.semaphore(name))

        w0_hi, w0_lo = sb("w0_hi", [P, H1], F32R), sb("w0_lo", [P, H1], F32R)
        w1_hi, w1_lo = sb("w1_hi", [P, CHUNKS, H1], F32R), sb("w1_lo", [P, CHUNKS, H1], F32R)
        w2_hi, w2_lo = sb("w2_hi", [P, M1, H2], F32R), sb("w2_lo", [P, M1, H2], F32R)
        w3_hi, w3_lo = sb("w3_hi", [P, M2, H3], F32R), sb("w3_lo", [P, M2, H3], F32R)
        stage = sb("stage", [P, 2, UNIT], F32)
        wo = sb("wo", [P, M3], F32)
        dw = sb("dw", [AUG, 2 * DIM + 1], F32)
        emb = sb("emb", [P, CHUNKS, GT, PAIR], F32)
        base = sb("base", [P, 1, FEATURES], I32)
        rows_all = sb("rows_all", [P, TILES + GT, FEATURES], I32)
        rows = sb("rows", [P, GT, FEATURES], I32)
        ident = sb("ident", [P, P], F32)
        dense = sb("dense", [AUG, N], F32)
        x_hi, x_lo = sb("x_hi", [P, 2, N], F32R), sb("x_lo", [P, 2, N], F32R)
        h1_hi, h1_lo = sb("h1_hi", [P, 2, 2 * N], F32R), sb("h1_lo", [P, 2, 2 * N], F32R)
        h2_hi, h2_lo = sb("h2_hi", [P, 2, 2 * N], F32R), sb("h2_lo", [P, 2, 2 * N], F32R)
        h3 = sb("h3", [P, M3 * N], F32)
        idx_f = h3[:, 0:TILES * FEATURES].rearrange("p (t f) -> p t f", f=FEATURES)
        junk = sb("junk", [P, 4 * P], mybir.dt.bfloat16)
        part = sb("part", [P, GT, NB + 1, PAIR], F32)
        sum_pair = sb("sum_pair", [P, GT, PAIR], F32)
        sum_e = sb("sum_e", [P, GT, DIM], F32)
        lin_parts = sb("lin_parts", [P, TILES, 2], F32)
        linear = sb("linear", [P, TILES], F32)
        sq_parts = sb("sq_parts", [P, TILES, NB + 1], F32)
        sq = sb("sq", [P, TILES], F32)
        sum_sq = sb("sum_sq", [P, TILES], F32)
        deep = sb("deep", [P, TILES], F32)
        y = sb("y", [P, TILES], F32)

        acc1 = ctx.enter_context(nc.psum_tensor("acc1", [P, M1 // 2, BANK], F32))
        acc2 = ctx.enter_context(nc.psum_tensor("acc2", [P, M2 // 2, BANK], F32))
        tp = ctx.enter_context(nc.psum_tensor("tp", [P, 2, BANK], F32))

        s_idx = sem("idx_landed")
        s_const = sem("const_landed")
        s_base = sem("base_ready")
        s_ident = sem("ident_ready")
        s_calc = sem("rows_chain")
        s_rows_all = sem("rows_all_ready")
        s_rows = sem("rows_copied")
        s_go = sem("gathers_released")
        s_chunk = [sem(f"chunk_landed{c}") for c in range(CHUNKS)]
        s_dense = sem("dense_landed")
        s_stage = [sem(f"stage_landed{i}") for i in range(2)]
        s_whi = sem("weights_hi")
        s_wlo = sem("weights_lo")
        s_t = sem("transposed")
        s_xhi = sem("x_hi_ready")
        s_xlo = sem("x_lo_ready")
        s_xused = sem("x_used")
        s_sq = sem("squares_done")
        s_free = sem("block_free")
        s_part = sem("parts_done")
        s_sum = sem("sums_done")
        s_sumsq = sem("sum_squares_done")
        s_l1, s_h1hi, s_h1lo, s_h1used = sem("l1_done"), sem("h1_hi_ready"), sem("h1_lo_ready"), sem("h1_used")
        s_l2, s_h2hi, s_h2lo = sem("l2_done"), sem("h2_hi_ready"), sem("h2_lo_ready")
        s_l3, s_h3, s_l4, s_deep = sem("l3_done"), sem("h3_ready"), sem("l4_done"), sem("deep_copied")
        s_y = sem("y_chain")
        s_out = sem("out_landed")

        w1_chunks = w1[DIM:, :].rearrange("(c p) n -> c p n", p=P)
        w2_pairs = w2.rearrange("(u k p) n -> u p k n", p=P, k=UNIT // H2)
        w3_all = w3.rearrange("(k p) n -> p k n", p=P)

        def unit_split(n):
            if n == 0:
                return w0_hi[:, :], w0_lo[:, :]
            if n <= CHUNKS:
                return w1_hi[:, n - 1, :], w1_lo[:, n - 1, :]
            k = (n - 1 - CHUNKS) * (UNIT // H2)
            if k < M1:
                return tuple(w[:, k:k + UNIT // H2, :].rearrange("p k n -> p (k n)") for w in (w2_hi, w2_lo))
            return tuple(w[:, :, :].rearrange("p k n -> p (k n)") for w in (w3_hi, w3_lo))

        def landed_units(n):
            return 16 * (n // 2 + 1) + (16 if n % 2 == 0 else 0)

        block = ctx.enter_context(nc.Block())

        @block.sync
        def _(sp):
            sp.dma_start(rows_all[:, 0:TILES, :], idx.rearrange("(p t) f -> p t f", t=TILES)).then_inc(s_idx, 16)
            sp.dma_start(dw[:, :], dense_w).then_inc(s_const, 16)
            sp.dma_start(wo[:, :], w_out).then_inc(s_const, 16)
            sp.dma_start(dense[:, :], dense_t[0, :, :]).then_inc(s_dense, 16)
            for n in range(UNITS):
                if n >= 2:
                    sp.wait_ge(s_wlo, n - 1)
                if n == 0:
                    for half in range(2):
                        sp.dma_start(stage[half * DIM:(half + 1) * DIM, 0, :], w1[0:DIM, :]).then_inc(s_stage[0], 16)
                    continue
                if n <= CHUNKS:
                    to, src = stage[:, n % 2, :], w1_chunks[n - 1]
                elif n < UNITS - 1:
                    to = stage[:, n % 2, :].rearrange("p (k n) -> p k n", n=H2)
                    src = w2_pairs[n - 1 - CHUNKS]
                else:
                    to, src = stage[:, n % 2, :].rearrange("p (k n) -> p k n", n=H3), w3_all
                sp.dma_start(to, src).then_inc(s_stage[n % 2], 16)
            with sp.Fori(1, GROUPS) as g:
                sp.wait_ge(s_t, STEPS * (g - 1) + 1)
                sp.dma_start(dense[:, :], dense_t[bass.ds(g, 1), :, :].rearrange("g a n -> (g a) n")).then_inc(s_dense, 16)
            sp.wait_ge(s_y, 5)
            sp.dma_start(out.rearrange("(p t) o -> p (t o)", t=TILES), y[:, :]).then_inc(s_out, 16)
            sp.wait_ge(s_out, 16)

        @block.gpsimd
        def _(pool):
            pool.iota(base[:, :, :], pattern=[[VOCAB, FEATURES]], base=0,
                      channel_multiplier=0).then_inc(s_base, 1)
            pool.memset(ident[:, :], 0.0).then_inc(s_ident, 1)
            pool.wait_ge(s_ident, 1)
            pool.affine_select(out=ident[:, :], in_=ident[:, :], compare_op=ALU.not_equal, fill=1.0, base=0,
                               pattern=[[-1, P]], channel_multiplier=1).then_inc(s_ident, 1)

            def gather_group(g, first):
                for c in range(CHUNKS):
                    if c == 0:
                        pool.wait_ge(s_rows, 2 * g + 1)
                    if c == ROWS_CUT:
                        pool.wait_ge(s_rows, 2 * g + 2)
                    for b, (c0, c1) in enumerate(BLOCKS):
                        if c == c0 and not first:
                            pool.wait_ge(s_free, NB * (g - 1) + b + 1)
                    if not first and (c in (0, ROWS_CUT) or c in [c0 for c0, _ in BLOCKS]):
                        pool.sem_inc(s_go, 1)
                    for t in range(GT):
                        for f in range(FPC):
                            pool.indirect_dma_start(
                                out=emb[:, c, t, f * ROW:(f + 1) * ROW], out_offset=None, in_=table[:, :],
                                in_offset=bass.IndirectOffsetOnAxis(ap=rows[:, t, FPC * c + f:FPC * c + f + 1], axis=0),
                            ).then_inc(s_chunk[c], 16)

            gather_group(0, True)
            with pool.Fori(1, GROUPS) as g:
                gather_group(g, False)

        @block.scalar
        def _(act):
            def split_weights(n):
                act.wait_ge(s_stage[n % 2], landed_units(n))
                nc.scalar.activation(unit_split(n)[0], stage[:, n % 2, :], ACT.Copy).then_inc(s_whi, 1)

            def copy_rows(g, cut):
                f = slice(0, FPC * ROWS_CUT) if cut == 0 else slice(FPC * ROWS_CUT, FEATURES)
                nc.scalar.activation(rows[:, :, f], rows_all[:, bass.ds(GT * g, GT), f], ACT.Copy).then_inc(s_rows, 1)

            def square(before, x, total):
                if not (isinstance(before, int) and before == 0):
                    act.wait_ge(s_sq, before)
                shape = junk[:, 0:x.shape[1] * (x.shape[2] if len(x.shape) == 3 else 1)]
                if len(x.shape) == 3:
                    shape = shape.rearrange("p (c d) -> p c d", d=x.shape[2])
                nc.scalar.activation(shape, x, ACT.Square, accum_out=total).then_inc(s_sq, 1)

            def squares(g, b):
                c0, c1 = BLOCKS[b]
                for c in range(c0, c1):
                    act.wait_ge(s_chunk[c], 64 * (g + 1))
                for t in range(GT):
                    square(SQUARES * g + GT * (b + 1) + t, emb[:, c0:c1, t, EMB],
                           sq_parts[:, bass.ds(GT * g + t, 1), b:b + 1].rearrange("p t b -> p (t b)"))

            def dense_step(g, first):
                act.wait_ge(s_t, STEPS * g + 1)
                for t in range(GT):
                    square(t if first else SQUARES * g - GT + t, tp[:, 0, N + t * ROW:N + t * ROW + DIM],
                           sq_parts[:, bass.ds(GT * g + t, 1), NB:NB + 1].rearrange("p t b -> p (t b)"))
                nc.scalar.activation(x_hi[:, 0, :], tp[:, 0, 0:N], ACT.Copy).then_inc(s_xhi, 1)

            def chunk_step(g, c):
                j = c + 1
                act.wait_ge(s_t, STEPS * g + j + 1)
                if j >= 2:
                    act.wait_ge(s_xused, CHUNKS * g + j - 1)
                nc.scalar.activation(x_hi[:, j % 2, :], tp[:, j % 2, 0:N], ACT.Copy).then_inc(s_xhi, 1)
                for b, (c0, c1) in enumerate(BLOCKS[:-1]):
                    if c == c1 - 1:
                        squares(g, b)

            def hidden1(g):
                for b in range(M1 // 2):
                    act.wait_ge(s_l1, M1 // 2 * g + b + 1)
                    if b >= 2:
                        act.wait_ge(s_h1used, (M1 // 2 - 1) * g + b - 1)
                    nc.scalar.activation(h1_hi[:, b % 2, :], acc1[:, b, :], ACT.Relu).then_inc(s_h1hi, 1)

            def hidden23(g):
                for b in range(M2 // 2):
                    act.wait_ge(s_l2, M2 // 2 * g + b + 1)
                    nc.scalar.activation(h2_hi[:, b, :], acc2[:, b, :], ACT.Relu).then_inc(s_h2hi, 1)
                act.wait_ge(s_l3, g + 1)
                nc.scalar.activation(h3[:, :], acc1[:, 0, :], ACT.Relu).then_inc(s_h3, 1)

            def sum_squares(g, before):
                act.wait_ge(s_sum, g + 1)
                for t in range(GT):
                    square(before + t, sum_e[:, t, :], sum_sq[:, bass.ds(GT * g + t, 1)])
                act.wait_ge(s_sq, before + GT)
                nc.scalar.activation(lin_parts[:, bass.ds(GT * g, GT), :], sum_pair[:, :, 0:PAIR:PAIR - 1],
                                     ACT.Copy).then_inc(s_sumsq, 1)

            def end_group(g):
                hidden1(g)
                squares(g, NB - 1)
                act.wait_ge(s_chunk[CHUNKS - 1], 64 * (g + 1))
                copy_rows(g + 1, 1)

            act.wait_ge(s_rows_all, 1)
            copy_rows(0, 0)
            copy_rows(0, 1)
            for n in range(3):
                split_weights(n)
            dense_step(0, True)
            for c in range(CHUNKS):
                chunk_step(0, c)
                if c == ROWS_CUT + 1:
                    act.wait_ge(s_rows_all, 2)
                    for cc in range(ROWS_CUT):
                        act.wait_ge(s_chunk[cc], 64)
                    copy_rows(1, 0)
                for n in (range(c + 3, c + 4) if c < CHUNKS - 1 else range(c + 3, UNITS)):
                    split_weights(n)
            end_group(0)
            with act.Fori(1, GROUPS) as g:
                dense_step(g, False)
                chunk_step(g, 0)
                hidden23(g - 1)
                sum_squares(g - 1, SQUARES * g)
                for c in range(1, CHUNKS):
                    chunk_step(g, c)
                    if c == ROWS_CUT + 1:
                        for cc in range(ROWS_CUT):
                            act.wait_ge(s_chunk[cc], 64 * (g + 1))
                        copy_rows(g + 1, 0)
                end_group(g)
            sum_squares(GROUPS - 1, SQUARES * GROUPS - GT)
            hidden23(GROUPS - 1)

        @block.vector
        def _(dve):
            def split_weights(n):
                dve.wait_ge(s_whi, n + 1)
                hi, lo = unit_split(n)
                nc.vector.tensor_tensor(lo, stage[:, n % 2, :], hi.bitcast(F32), ALU.subtract).then_inc(s_wlo, 1)

            def number_rows(tiles, k):
                f, i = idx_f[:, tiles, :], rows_all[:, tiles, :]
                nc.vector.tensor_scalar(f, i, 0.0, float(VOCAB), ALU.is_lt, ALU.mult).then_inc(s_calc, 1)
                dve.wait_ge(s_calc, k + 1)
                nc.vector.tensor_tensor(f, i, f, ALU.add).then_inc(s_calc, 1)
                dve.wait_ge(s_calc, k + 2)
                nc.vector.tensor_scalar(f, f, 0.0, float(VOCAB - 1), ALU.max, ALU.min).then_inc(s_calc, 1)
                dve.wait_ge(s_calc, k + 3)
                nc.vector.tensor_tensor(i, f, base[:, :, :].to_broadcast([P, tiles.stop - tiles.start, FEATURES]), ALU.add).then_inc(s_rows_all, 1)

            def rest(lo, psum, hi, relu=False):
                if relu:
                    return nc.vector.scalar_tensor_tensor(lo, psum, 0.0, hi.bitcast(F32), ALU.max, ALU.subtract)
                return nc.vector.tensor_tensor(lo, psum, hi.bitcast(F32), ALU.subtract)

            def dense_step(g):
                dve.wait_ge(s_xhi, STEPS * g + 1)
                nc.vector.tensor_copy(
                    part[:, :, NB, ROW:PAIR], tp[:, 0, N:N + GT * ROW].rearrange("p (t d) -> p t d", d=ROW))
                rest(x_hi[DIM:P, 0, :], tp[DIM:P, 0, 0:N], x_hi[DIM:P, 0, :]).then_inc(s_xlo, 1)

            def block_sums(g, b):
                c0, c1 = BLOCKS[b]
                dve.wait_ge(s_sq, SQUARES * g + GT * (b + 2))
                nc.vector.tensor_reduce(
                    part[:, :, b, :], emb[:, c0:c1, :, :].rearrange("p c t d -> p t d c"),
                    AX.X, ALU.add).then_inc(s_free, 1)

            def chunk_step(g, c):
                j = c + 1
                dve.wait_ge(s_xhi, STEPS * g + j + 1)
                rest(x_lo[:, j % 2, :], tp[:, j % 2, 0:N], x_hi[:, j % 2, :]).then_inc(s_xlo, 1)
                for b, (c0, c1) in enumerate(BLOCKS[:-1]):
                    if c == c1 - 1:
                        block_sums(g, b)

            def hidden1(g):
                for b in range(M1 // 2):
                    dve.wait_ge(s_h1hi, M1 // 2 * g + b + 1)
                    rest(h1_lo[:, b % 2, :], acc1[:, b, :], h1_hi[:, b % 2, :], True).then_inc(s_h1lo, 1)

            def hidden2(g):
                for b in range(M2 // 2):
                    dve.wait_ge(s_h2hi, M2 // 2 * g + b + 1)
                    rest(h2_lo[:, b, :], acc2[:, b, :], h2_hi[:, b, :], True).then_inc(s_h2lo, 1)

            def copy_deep(g):
                dve.wait_ge(s_l4, g + 1)
                nc.vector.tensor_copy(deep[:, bass.ds(GT * g, GT)], acc2[:, 0, 0:GT]).then_inc(s_deep, 1)

            def end_group(g, first):
                hidden1(g)
                block_sums(g, NB - 1)
                dve.wait_ge(s_free, NB * (g + 1))
                if not first:
                    dve.wait_ge(s_sumsq, g)
                nc.vector.tensor_reduce(
                    sum_pair[:, :, :], part[:, :, :, :].rearrange("p t n d -> p t d n"),
                    AX.X, ALU.add).then_inc(s_part, 1)
                dve.wait_ge(s_part, g + 1)
                nc.vector.tensor_tensor(sum_e[:, :, :], sum_pair[:, :, 1:1 + DIM], sum_pair[:, :, ROW:ROW + DIM],
                                        ALU.add).then_inc(s_sum, 1)

            nc.vector.memset(part[:, :, NB, 0:ROW], 0.0)
            nc.vector.memset(rows_all[:, TILES:TILES + GT, :], 0)
            dve.wait_ge(s_idx, 16)
            dve.wait_ge(s_base, 1)
            number_rows(slice(0, GT), 0)
            number_rows(slice(GT, TILES), 3)
            for n in range(3):
                split_weights(n)
            dense_step(0)
            for c in range(CHUNKS):
                chunk_step(0, c)
                for n in (range(c + 3, c + 4) if c < CHUNKS - 1 else range(c + 3, UNITS)):
                    split_weights(n)
            end_group(0, True)
            with dve.Fori(1, GROUPS) as g:
                dense_step(g)
                chunk_step(g, 0)
                hidden2(g - 1)
                copy_deep(g - 1)
                for c in range(1, CHUNKS):
                    chunk_step(g, c)
                end_group(g, False)
            nc.vector.tensor_reduce(sq[:, :], sq_parts[:, :, :], AX.X, ALU.add).then_inc(s_y, 1)
            dve.wait_ge(s_sumsq, GROUPS)
            nc.vector.tensor_reduce(linear[:, :], lin_parts[:, :, :], AX.X, ALU.add).then_inc(s_y, 1)
            dve.wait_ge(s_y, 2)
            nc.vector.tensor_tensor(sum_sq[:, :], sum_sq[:, :], sq[:, :], ALU.subtract).then_inc(s_y, 1)
            dve.wait_ge(s_y, 3)
            nc.vector.scalar_tensor_tensor(linear[:, :], sum_sq[:, :], 0.5, linear[:, :], ALU.mult, ALU.add).then_inc(s_y, 1)
            hidden2(GROUPS - 1)
            copy_deep(GROUPS - 1)
            dve.wait_ge(s_y, 4)
            dve.wait_ge(s_deep, GROUPS)
            nc.vector.tensor_tensor(y[:, :], linear[:, :], deep[:, :], ALU.add).then_inc(s_y, 1)

        @block.tensor
        def _(pe):
            def product(bank, m, hi, lo, cols, x, x_rest, start, stop):
                to = bank[:, m % 2 * N:(m % 2 + 1) * N]
                for i, (w, v) in enumerate(((lo, x), (hi, x_rest), (hi, x))):
                    last = nc.tensor.matmul(to, w[:, cols], v, start=start and m % 2 == 0 and i == 0,
                                            stop=stop and i == 2, skip_group_check=True)
                return last

            def dense_load(g):
                pe.wait_ge(s_dense, 16 * (g + 1))
                nc.tensor.matmul(tp[:, 0, 0:N], dw[:, 0:P], dense[:, :], start=True, stop=True)
                for t in range(GT):
                    last = nc.tensor.matmul(tp[:, 0, N + t * ROW:N + (t + 1) * ROW], dense[:, t * P:(t + 1) * P],
                                            dw[:, DIM:P + 1], start=True, stop=True)
                last.then_inc(s_t, 1)

            def dense_product(g, ms):
                for m in ms:
                    to = acc1[:, m // 2, m % 2 * N:(m % 2 + 1) * N]
                    for i, w in enumerate((w0_lo, w0_hi)):
                        last = nc.tensor.matmul(to, w[:, m * P:(m + 1) * P], x_hi[:, 0, :],
                                                start=m % 2 == 0 and i == 0, stop=False, skip_group_check=True)
                return last

            def transpose_chunk(g, c):
                j = c + 1
                pe.wait_ge(s_chunk[c], 64 * (g + 1))
                for t in range(GT):
                    last = nc.tensor.transpose(tp[:, j % 2, t * P:(t + 1) * P], emb[:, c, t, EMB], ident[:, :])
                last.then_inc(s_t, 1)

            def chunk_product(g, c, first):
                j = c + 1
                if first:
                    pe.wait_ge(s_wlo, c + 2)
                pe.wait_ge(s_xlo, STEPS * g + j + 1)
                for m in range(M1):
                    if m == 3 and c + 1 < CHUNKS:
                        transpose_chunk(g, c + 1)
                    last = product(acc1[:, m // 2, :], m, w1_hi[:, c, :], w1_lo[:, c, :], slice(m * P, (m + 1) * P),
                                   x_hi[:, j % 2, :], x_lo[:, j % 2, :], False, c == CHUNKS - 1)
                    if c == CHUNKS - 1 and m % 2 == 1:
                        last.then_inc(s_l1, 1)
                if c < CHUNKS - 1:
                    last.then_inc(s_xused, 1)

            def layer2(g, first):
                if not first:
                    pe.wait_ge(s_deep, g)
                for k in range(M1):
                    b = k // 2
                    if k % 2 == 0:
                        pe.wait_ge(s_h1lo, M1 // 2 * g + b + 1)
                    x = slice(k % 2 * N, (k % 2 + 1) * N)
                    for m in range(M2):
                        last = product(acc2[:, m // 2, :], m, w2_hi[:, k, :], w2_lo[:, k, :], slice(m * P, (m + 1) * P),
                                       h1_hi[:, b % 2, x], h1_lo[:, b % 2, x], k == 0, k == M1 - 1)
                        if k == M1 - 1 and m % 2 == 1:
                            last.then_inc(s_l2, 1)
                        elif k % 2 == 1 and m == M2 - 1:
                            last.then_inc(s_h1used, 1)

            def layer3(g):
                for k in range(M2):
                    b = k // 2
                    if k % 2 == 0:
                        pe.wait_ge(s_h2lo, M2 // 2 * g + b + 1)
                    x = slice(k % 2 * N, (k % 2 + 1) * N)
                    for m in range(M3):
                        last = product(acc1[:, 0, :], m, w3_hi[:, k, :], w3_lo[:, k, :], slice(m * P, (m + 1) * P),
                                       h2_hi[:, b, x], h2_lo[:, b, x], k == 0, k == M2 - 1)
                last.then_inc(s_l3, 1)

            def layer4(g):
                for t in range(GT):
                    for k in range(M3):
                        last = nc.tensor.matmul(acc2[:, 0, t:t + 1], h3[:, k * N + t * P:k * N + (t + 1) * P],
                                                wo[:, k:k + 1], start=(k == 0), stop=(k == M3 - 1))
                last.then_inc(s_l4, 1)

            pe.wait_ge(s_const, 32)
            pe.wait_ge(s_ident, 2)
            dense_load(0)
            transpose_chunk(0, 0)
            pe.wait_ge(s_wlo, 1)
            pe.wait_ge(s_xlo, 1)
            dense_product(0, range(M1)).then_inc(s_xused, 1)
            for c in range(CHUNKS):
                chunk_product(0, c, True)
            pe.wait_ge(s_wlo, UNITS)
            with pe.Fori(1, GROUPS) as g:
                dense_load(g)
                transpose_chunk(g, 0)
                layer2(g - 1, False)
                pe.wait_ge(s_xlo, STEPS * g + 1)
                dense_product(g, range(4, M1))
                layer3(g - 1)
                dense_product(g, range(2, 4))
                pe.wait_ge(s_h3, g)
                dense_product(g, range(0, 2)).then_inc(s_xused, 1)
                layer4(g - 1)
                for c in range(CHUNKS):
                    chunk_product(g, c, False)
            layer2(GROUPS - 1, False)
            layer3(GROUPS - 1)
            pe.wait_ge(s_h3, GROUPS)
            layer4(GROUPS - 1)


def kernel(**inputs):
    import numpy as np
    import concourse.bacc as bacc
    from concourse.bass_utils import run_bass_kernel_spmd as run

    a = {k: np.asarray(v) for k, v in inputs.items()}
    emb, lin = a["L0_rec_emb_tables"], a["L0_rec_lin_tables"]
    table = np.empty((FEATURES, VOCAB, ROW), np.float32)
    table[0::2, :, 0], table[0::2, :, 1:] = lin[0::2], emb[0::2]
    table[1::2, :, :DIM], table[1::2, :, DIM] = emb[1::2], lin[1::2]
    table = table.reshape(-1, ROW)
    ones = np.ones((BATCH, 2), np.float32)
    x = np.concatenate([a["r_dense"], ones], axis=1).reshape(P, GROUPS, GT, AUG)
    dense_t = np.ascontiguousarray(x.transpose(1, 3, 2, 0)).reshape(GROUPS, AUG, N)
    dense_w = np.zeros((AUG, 2 * DIM + 1), np.float32)
    dense_w[:13, 0:DIM] = a["L0_rec_Wd"]
    dense_w[:13, DIM:2 * DIM] = a["L0_rec_Wd"]
    dense_w[:13, 2 * DIM:] = a["L0_rec_Wld"]
    dense_w[13, 2 * DIM] = a["L0_rec_bld"][0]
    dense_w[14, 2 * DIM] = a["L0_rec_bias"][0, 0]
    w_out = np.ascontiguousarray(a["L0_rec_Wout"].reshape(M3, P).T)
    arrays = {"table": table, "idx": a["r_sparse_idx"], "dense_t": dense_t, "dense_w": dense_w,
              "w1": a["L0_rec_W1"], "w2": a["L0_rec_W2"], "w3": a["L0_rec_W3"], "w_out": w_out}
    arrays = {k: np.ascontiguousarray(v) for k, v in arrays.items()}

    nc = bacc.Bacc("TRN2", target_bir_lowering=False, num_devices=1)
    args = [nc.dram_tensor(k, v.shape, mybir.dt.from_np(v.dtype), kind="ExternalInput").ap() for k, v in arrays.items()]
    out = nc.dram_tensor("y_out", (BATCH, 1), F32, kind="ExternalOutput").ap()
    deepfm(nc, *args, out)
    return run(nc, [arrays], core_ids=[0]).results[0]["y_out"]
```

```python
from contextlib import ExitStack

import concourse.bass as bass
from concourse import mybir

F32 = mybir.dt.float32
F32R = mybir.dt.float32r
I32 = mybir.dt.int32
ALU = mybir.AluOpType
ACT = mybir.ActivationFunctionType
AX = mybir.AxisListType

P = 128
BATCH, FEATURES, VOCAB, DIM = 2048, 26, 12500, 64
H1, H2, H3 = 1024, 512, 256
ROW = DIM + 1
AUG = 13 + 2
TILES = BATCH // P
GT = 2
N = GT * P
GROUPS = TILES // GT
CHUNKS = FEATURES * DIM // P
FPC = P // DIM
PAIR = FPC * ROW
EMB = slice(1, 1 + P)
M1, M2, M3 = H1 // P, H2 // P, H3 // P
UNIT = 1024
BLOCKS = [(0, 3), (3, 6), (6, 9), (9, 13)]
NB = len(BLOCKS)
LANDED = 16 * GT * FPC
SQUARES = GT * (NB + 2)
STEPS = CHUNKS + 1
ROWS_CUT = 7
UNITS = 1 + CHUNKS + H1 * H2 // P // UNIT + H2 * H3 // P // UNIT
BANK = 512


def deepfm(nc, table, idx, dense_t, dense_w, w1, w2, w3, w_out, out):
    ctx = ExitStack()
    with ctx:
        def sb(name, shape, dt):
            return ctx.enter_context(nc.sbuf_tensor(name, shape, dt))

        def sem(name):
            return ctx.enter_context(nc.semaphore(name))

        w0_hi, w0_lo = sb("w0_hi", [P, H1], F32R), sb("w0_lo", [P, H1], F32R)
        w1_hi, w1_lo = sb("w1_hi", [P, CHUNKS, H1], F32R), sb("w1_lo", [P, CHUNKS, H1], F32R)
        w2_hi, w2_lo = sb("w2_hi", [P, M1, H2], F32R), sb("w2_lo", [P, M1, H2], F32R)
        w3_hi, w3_lo = sb("w3_hi", [P, M2, H3], F32R), sb("w3_lo", [P, M2, H3], F32R)
        stage = sb("stage", [P, 2, UNIT], F32)
        wo = sb("wo", [P, M3], F32)
        dw = sb("dw", [AUG, 2 * DIM + 1], F32)
        emb = sb("emb", [P, CHUNKS, GT, PAIR], F32)
        base = sb("base", [P, 1, FEATURES], I32)
        rows_all = sb("rows_all", [P, TILES + GT, FEATURES], I32)
        rows = sb("rows", [P, GT, FEATURES], I32)
        ident = sb("ident", [P, P], F32)
        dense = sb("dense", [AUG, N], F32)
        x_hi, x_lo = sb("x_hi", [P, 2, N], F32R), sb("x_lo", [P, 2, N], F32R)
        h1_hi, h1_lo = sb("h1_hi", [P, 2, 2 * N], F32R), sb("h1_lo", [P, 2, 2 * N], F32R)
        h2_hi, h2_lo = sb("h2_hi", [P, 2, 2 * N], F32R), sb("h2_lo", [P, 2, 2 * N], F32R)
        h3 = sb("h3", [P, M3 * N], F32)
        idx_f = h3[:, 0:TILES * FEATURES].rearrange("p (t f) -> p t f", f=FEATURES)
        junk = sb("junk", [P, 4 * P], mybir.dt.bfloat16)
        part = sb("part", [P, GT, NB + 1, PAIR], F32)
        sum_pair = sb("sum_pair", [P, GT, PAIR], F32)
        sum_e = sb("sum_e", [P, GT, DIM], F32)
        lin_parts = sb("lin_parts", [P, TILES, 2], F32)
        linear = sb("linear", [P, TILES], F32)
        sq_parts = sb("sq_parts", [P, TILES, NB + 1], F32)
        sq = sb("sq", [P, TILES], F32)
        sum_sq = sb("sum_sq", [P, TILES], F32)
        deep = sb("deep", [P, TILES], F32)
        y = sb("y", [P, TILES], F32)

        acc1 = ctx.enter_context(nc.psum_tensor("acc1", [P, M1 // 2, BANK], F32))
        acc2 = ctx.enter_context(nc.psum_tensor("acc2", [P, M2 // 2, BANK], F32))
        tp = ctx.enter_context(nc.psum_tensor("tp", [P, 2, BANK], F32))

        s_idx = sem("idx_landed")
        s_const = sem("const_landed")
        s_base = sem("base_ready")
        s_ident = sem("ident_ready")
        s_calc = sem("rows_chain")
        s_rows_all = sem("rows_all_ready")
        s_rows = sem("rows_copied")
        s_go = sem("gathers_released")
        s_chunk = [sem(f"chunk_landed{c}") for c in range(CHUNKS)]
        s_dense = sem("dense_landed")
        s_stage = [sem(f"stage_landed{i}") for i in range(2)]
        s_whi = sem("weights_hi")
        s_wlo = sem("weights_lo")
        s_t = sem("transposed")
        s_xhi = sem("x_hi_ready")
        s_xlo = sem("x_lo_ready")
        s_xused = sem("x_used")
        s_sq = sem("squares_done")
        s_free = sem("block_free")
        s_part = sem("parts_done")
        s_sum = sem("sums_done")
        s_sumsq = sem("sum_squares_done")
        s_l1, s_h1hi, s_h1lo, s_h1used = sem("l1_done"), sem("h1_hi_ready"), sem("h1_lo_ready"), sem("h1_used")
        s_l2, s_h2hi, s_h2lo = sem("l2_done"), sem("h2_hi_ready"), sem("h2_lo_ready")
        s_l3, s_h3, s_l4, s_deep = sem("l3_done"), sem("h3_ready"), sem("l4_done"), sem("deep_copied")
        s_y = sem("y_chain")
        s_out = sem("out_landed")

        w1_chunks = w1[DIM:, :].rearrange("(c p) n -> c p n", p=P)
        w2_pairs = w2.rearrange("(u k p) n -> u p k n", p=P, k=UNIT // H2)
        w3_all = w3.rearrange("(k p) n -> p k n", p=P)

        def unit_split(n):
            if n == 0:
                return w0_hi[:, :], w0_lo[:, :]
            if n <= CHUNKS:
                return w1_hi[:, n - 1, :], w1_lo[:, n - 1, :]
            k = (n - 1 - CHUNKS) * (UNIT // H2)
            if k < M1:
                return tuple(w[:, k:k + UNIT // H2, :].rearrange("p k n -> p (k n)") for w in (w2_hi, w2_lo))
            return tuple(w[:, :, :].rearrange("p k n -> p (k n)") for w in (w3_hi, w3_lo))

        READY_UNITS = 3

        def units_behind(c):
            return range(min(UNITS, READY_UNITS + (3 * c + 1) // 2), min(UNITS, READY_UNITS + (3 * c + 4) // 2))

        def landed_units(n):
            return 16 * (n // 2 + 1) + (16 if n % 2 == 0 else 0)

        block = ctx.enter_context(nc.Block())

        @block.sync
        def _(sp):
            sp.dma_start(rows_all[:, 0:TILES, :], idx.rearrange("(p t) f -> p t f", t=TILES)).then_inc(s_idx, 16)
            sp.dma_start(dw[:, :], dense_w).then_inc(s_const, 16)
            sp.dma_start(wo[:, :], w_out).then_inc(s_const, 16)
            sp.dma_start(dense[:, :], dense_t[0, :, :]).then_inc(s_dense, 16)
            for n in range(UNITS):
                if n >= 2:
                    sp.wait_ge(s_wlo, n - 1)
                if n == 0:
                    for half in range(2):
                        sp.dma_start(stage[half * DIM:(half + 1) * DIM, 0, :], w1[0:DIM, :]).then_inc(s_stage[0], 16)
                    continue
                if n <= CHUNKS:
                    to, src = stage[:, n % 2, :], w1_chunks[n - 1]
                elif n < UNITS - 1:
                    to = stage[:, n % 2, :].rearrange("p (k n) -> p k n", n=H2)
                    src = w2_pairs[n - 1 - CHUNKS]
                else:
                    to, src = stage[:, n % 2, :].rearrange("p (k n) -> p k n", n=H3), w3_all
                sp.dma_start(to, src).then_inc(s_stage[n % 2], 16)
            with sp.Fori(1, GROUPS) as g:
                sp.wait_ge(s_t, STEPS * (g - 1) + 1)
                sp.dma_start(dense[:, :], dense_t[bass.ds(g, 1), :, :].rearrange("g a n -> (g a) n")
                             ).then_inc(s_dense, 16)
            sp.wait_ge(s_y, 5)
            sp.dma_start(out.rearrange("(p t) o -> p (t o)", t=TILES), y[:, :]).then_inc(s_out, 16)
            sp.wait_ge(s_out, 16)

        @block.gpsimd
        def _(pool):
            pool.iota(base[:, :, :], pattern=[[VOCAB, FEATURES]], base=0,
                      channel_multiplier=0).then_inc(s_base, 1)
            pool.memset(ident[:, :], 0.0).then_inc(s_ident, 1)
            pool.wait_ge(s_ident, 1)
            pool.affine_select(out=ident[:, :], in_=ident[:, :], compare_op=ALU.not_equal, fill=1.0, base=0,
                               pattern=[[-1, P]], channel_multiplier=1).then_inc(s_ident, 1)

            def gather_chunk(c):
                for t in range(GT):
                    for f in range(FPC):
                        pool.indirect_dma_start(
                            out=emb[:, c, t, f * ROW:(f + 1) * ROW], out_offset=None, in_=table[:, :],
                            in_offset=bass.IndirectOffsetOnAxis(ap=rows[:, t, FPC * c + f:FPC * c + f + 1], axis=0),
                        ).then_inc(s_chunk[c], 16)

            def gather_group(g):
                for c in range(CHUNKS):
                    if c == 0:
                        pool.wait_ge(s_rows, 2 * g)
                    if c == ROWS_CUT:
                        pool.wait_ge(s_rows, 2 * g + 1)
                    for b, (c0, _) in enumerate(BLOCKS):
                        if c == c0:
                            pool.wait_ge(s_free, NB * (g - 1) + b + 1)
                    if c in (0, ROWS_CUT) or c in [c0 for c0, _ in BLOCKS]:
                        pool.sem_inc(s_go, 1)
                    gather_chunk(c)

            pool.wait_ge(s_rows, 1)
            for c in range(CHUNKS):
                gather_chunk(c)
            with pool.Fori(1, GROUPS - 1, 2) as g:
                gather_group(g)
                gather_group(g + 1)
            gather_group(GROUPS - 1)

        @block.scalar
        def _(act):
            def split_weights(n):
                act.wait_ge(s_stage[n % 2], landed_units(n))
                nc.scalar.activation(unit_split(n)[0], stage[:, n % 2, :], ACT.Copy).then_inc(s_whi, 1)

            def copy_rows(g, cut):
                f = slice(0, FPC * ROWS_CUT) if cut == 0 else slice(FPC * ROWS_CUT, FEATURES)
                nc.scalar.activation(rows[:, :, f], rows_all[:, bass.ds(GT * g, GT), f], ACT.Copy).then_inc(s_rows, 1)

            def square(before, x, total):
                if before is not None:
                    act.wait_ge(s_sq, before)
                shape = junk[:, 0:x.shape[1] * (x.shape[2] if len(x.shape) == 3 else 1)]
                if len(x.shape) == 3:
                    shape = shape.rearrange("p (c d) -> p c d", d=x.shape[2])
                nc.scalar.activation(shape, x, ACT.Square, accum_out=total).then_inc(s_sq, 1)

            def squares(g, b):
                c0, c1 = BLOCKS[b]
                for c in range(c0, c1):
                    act.wait_ge(s_chunk[c], LANDED * (g + 1))
                for i in range(GT):
                    square(SQUARES * g + GT + GT * b + i, emb[:, c0:c1, i, EMB],
                           sq_parts[:, bass.ds(GT * g + i, 1), b:b + 1].rearrange("p t b -> p (t b)"))

            def dense_step(g, first=False):
                act.wait_ge(s_t, STEPS * g + 1)
                for i in range(GT):
                    before = SQUARES * g - GT + i if not first else i if i > 0 else None
                    square(before, tp[:, 0, N + i * ROW:N + i * ROW + DIM],
                           sq_parts[:, bass.ds(GT * g + i, 1), NB:NB + 1].rearrange("p t b -> p (t b)"))
                nc.scalar.activation(x_hi[:, 0, 0:N], tp[:, 0, 0:N], ACT.Copy).then_inc(s_xhi, 1)

            def chunk_step(g, c):
                j = c + 1
                act.wait_ge(s_t, STEPS * g + j + 1)
                if j >= 2:
                    act.wait_ge(s_xused, CHUNKS * g + j - 1)
                nc.scalar.activation(x_hi[:, j % 2, 0:N], tp[:, j % 2, 0:N], ACT.Copy).then_inc(s_xhi, 1)
                for b, (c0, c1) in enumerate(BLOCKS[:-1]):
                    if c == c1 - 1:
                        squares(g, b)

            def hidden1(g, banks):
                for b in banks:
                    act.wait_ge(s_l1, M1 // 2 * g + b + 1)
                    if b >= 2:
                        act.wait_ge(s_h1used, (M1 // 2 - 1) * g + b - 1)
                    nc.scalar.activation(h1_hi[:, b % 2, :], acc1[:, b, :], ACT.Relu).then_inc(s_h1hi, 1)

            def hidden23(g):
                for b in range(M2 // 2):
                    act.wait_ge(s_l2, M2 // 2 * g + b + 1)
                    nc.scalar.activation(h2_hi[:, b, :], acc2[:, b, :], ACT.Relu).then_inc(s_h2hi, 1)
                act.wait_ge(s_l3, g + 1)
                nc.scalar.activation(h3[:, :], acc1[:, 0, :], ACT.Relu).then_inc(s_h3, 1)

            def sum_squares(g, before):
                act.wait_ge(s_sum, g + 1)
                for i in range(GT):
                    square(before + i, sum_e[:, i, :], sum_sq[:, bass.ds(GT * g + i, 1)])
                act.wait_ge(s_sq, before + GT)
                nc.scalar.activation(lin_parts[:, bass.ds(GT * g, GT), :], sum_pair[:, :, 0:PAIR:PAIR - 1],
                                     ACT.Copy).then_inc(s_sumsq, 1)

            def middle(g, last):
                dense_step(g)
                chunk_step(g, 0)
                hidden23(last)
                sum_squares(last, SQUARES * g)

            def copy_next_rows(g, c):
                if c == ROWS_CUT + 1:
                    for cc in range(ROWS_CUT):
                        act.wait_ge(s_chunk[cc], LANDED * (g + 1))
                    copy_rows(g + 1, 0)

            def end_group(g):
                hidden1(g, (0, 1))
                squares(g, NB - 1)
                copy_rows(g + 1, 1)
                hidden1(g, (2, 3))

            for n in range(READY_UNITS):
                split_weights(n)
            dense_step(0, True)
            act.wait_ge(s_rows_all, 1)
            for c in range(CHUNKS):
                chunk_step(0, c)
                copy_next_rows(0, c)
                for n in units_behind(c):
                    split_weights(n)
            end_group(0)
            with act.Fori(1, GROUPS) as g:
                middle(g, g - 1)
                for c in range(1, CHUNKS):
                    chunk_step(g, c)
                    copy_next_rows(g, c)
                end_group(g)
            sum_squares(GROUPS - 1, SQUARES * GROUPS - GT)
            hidden23(GROUPS - 1)

        @block.vector
        def _(dve):
            def split_weights(n):
                dve.wait_ge(s_whi, n + 1)
                hi, lo = unit_split(n)
                nc.vector.tensor_tensor(lo, stage[:, n % 2, :], hi.bitcast(F32), ALU.subtract).then_inc(s_wlo, 1)

            def number_rows(tiles, k, to, ready):
                f, i = idx_f[:, tiles, :], rows_all[:, tiles, :]
                nc.vector.tensor_scalar(f, i, 0.0, float(VOCAB), ALU.is_lt, ALU.mult).then_inc(s_calc, 1)
                dve.wait_ge(s_calc, k + 1)
                nc.vector.tensor_tensor(f, i, f, ALU.add).then_inc(s_calc, 1)
                dve.wait_ge(s_calc, k + 2)
                nc.vector.tensor_scalar(f, f, 0.0, float(VOCAB - 1), ALU.max, ALU.min).then_inc(s_calc, 1)
                dve.wait_ge(s_calc, k + 3)
                nc.vector.tensor_tensor(to, f, base[:, :, :].to_broadcast([P, tiles.stop - tiles.start, FEATURES]),
                                        ALU.add).then_inc(ready, 1)

            def rest(lo, psum, hi, relu=False):
                if relu:
                    return nc.vector.scalar_tensor_tensor(lo, psum, 0.0, hi.bitcast(F32), ALU.max, ALU.subtract)
                return nc.vector.tensor_tensor(lo, psum, hi.bitcast(F32), ALU.subtract)

            def dense_step(g):
                dve.wait_ge(s_xhi, STEPS * g + 1)
                nc.vector.tensor_copy(
                    part[:, :, NB, ROW:PAIR],
                    tp[:, 0, N:N + GT * ROW].rearrange("p (t d) -> p t d", d=ROW))
                x = x_hi[DIM:P, 0, 0:N]
                rest(x, tp[DIM:P, 0, 0:N], x).then_inc(s_xlo, 1)

            def block_sums(g, b):
                c0, c1 = BLOCKS[b]
                dve.wait_ge(s_sq, SQUARES * g + GT + GT * (b + 1))
                nc.vector.tensor_reduce(
                    part[:, :, b, :], emb[:, c0:c1, :, :].rearrange("p c t d -> p t d c"),
                    AX.X, ALU.add).then_inc(s_free, 1)

            def chunk_step(g, c):
                j = c + 1
                dve.wait_ge(s_xhi, STEPS * g + j + 1)
                rest(x_lo[:, j % 2, 0:N], tp[:, j % 2, 0:N], x_hi[:, j % 2, 0:N]).then_inc(s_xlo, 1)
                for b, (c0, c1) in enumerate(BLOCKS[:-1]):
                    if c == c1 - 1:
                        block_sums(g, b)

            def hidden1(g, banks):
                for b in banks:
                    dve.wait_ge(s_h1hi, M1 // 2 * g + b + 1)
                    rest(h1_lo[:, b % 2, :], acc1[:, b, :], h1_hi[:, b % 2, :],
                         True).then_inc(s_h1lo, 1)

            def hidden2(g):
                for b in range(M2 // 2):
                    dve.wait_ge(s_h2hi, M2 // 2 * g + b + 1)
                    rest(h2_lo[:, b, :], acc2[:, b, :], h2_hi[:, b, :], True).then_inc(s_h2lo, 1)

            def copy_deep(g):
                dve.wait_ge(s_l4, g + 1)
                nc.vector.tensor_copy(deep[:, bass.ds(GT * g, GT)], acc2[:, 0, 0:GT]).then_inc(s_deep, 1)

            def end_group(g, first=False):
                hidden1(g, (0, 1))
                block_sums(g, NB - 1)
                dve.wait_ge(s_free, NB * (g + 1))
                if not first:
                    dve.wait_ge(s_sumsq, g)
                nc.vector.tensor_reduce(
                    sum_pair[:, :, :], part[:, :, :, :].rearrange("p t n d -> p t d n"),
                    AX.X, ALU.add).then_inc(s_part, 1)
                dve.wait_ge(s_part, g + 1)
                nc.vector.tensor_tensor(sum_e[:, :, :], sum_pair[:, :, 1:1 + DIM],
                                        sum_pair[:, :, ROW:ROW + DIM], ALU.add).then_inc(s_sum, 1)
                hidden1(g, (2, 3))

            def middle(g, last):
                dense_step(g)
                chunk_step(g, 0)
                hidden2(last)
                copy_deep(last)

            nc.vector.memset(rows_all[:, TILES:TILES + GT, :], 0)
            nc.vector.memset(part[:, :, NB, 0:ROW], 0.0)
            dve.wait_ge(s_idx, 16)
            dve.wait_ge(s_base, 1)
            number_rows(slice(0, GT), 0, rows[:, :, :], s_rows)
            number_rows(slice(GT, TILES), 3, rows_all[:, GT:TILES, :], s_rows_all)
            for n in range(READY_UNITS):
                split_weights(n)
            dense_step(0)
            for c in range(CHUNKS):
                chunk_step(0, c)
                for n in units_behind(c):
                    split_weights(n)
            end_group(0, True)
            with dve.Fori(1, GROUPS) as g:
                middle(g, g - 1)
                for c in range(1, CHUNKS):
                    chunk_step(g, c)
                end_group(g)
            nc.vector.tensor_reduce(sq[:, :], sq_parts[:, :, :], AX.X, ALU.add).then_inc(s_y, 1)
            dve.wait_ge(s_sumsq, GROUPS)
            nc.vector.tensor_reduce(linear[:, :], lin_parts[:, :, :], AX.X, ALU.add).then_inc(s_y, 1)
            dve.wait_ge(s_y, 2)
            nc.vector.tensor_tensor(sum_sq[:, :], sum_sq[:, :], sq[:, :], ALU.subtract).then_inc(s_y, 1)
            dve.wait_ge(s_y, 3)
            nc.vector.scalar_tensor_tensor(linear[:, :], sum_sq[:, :], 0.5, linear[:, :],
                                           ALU.mult, ALU.add).then_inc(s_y, 1)
            hidden2(GROUPS - 1)
            copy_deep(GROUPS - 1)
            dve.wait_ge(s_y, 4)
            dve.wait_ge(s_deep, GROUPS)
            nc.vector.tensor_tensor(y[:, :], linear[:, :], deep[:, :], ALU.add).then_inc(s_y, 1)

        @block.tensor
        def _(pe):
            def product(bank, m, hi, lo, k, x, x_rest, start, stop):
                to = bank[:, m % 2 * N:m % 2 * N + N]
                for i, (w, v) in enumerate(((lo, x), (hi, x_rest), (hi, x))):
                    last = nc.tensor.matmul(to, w[:, k, m * P:(m + 1) * P], v, start=start and m % 2 == 0 and i == 0,
                                            stop=stop and i == 2, skip_group_check=True)
                return last

            def dense_load(g):
                pe.wait_ge(s_dense, 16 * (g + 1))
                nc.tensor.matmul(tp[:, 0, 0:N], dw[:, 0:P], dense[:, :], start=True, stop=True)
                for i in range(GT):
                    last = nc.tensor.matmul(tp[:, 0, N + i * ROW:N + (i + 1) * ROW], dense[:, i * P:(i + 1) * P],
                                            dw[:, DIM:P + 1], start=True, stop=True)
                last.then_inc(s_t, 1)

            def dense_product(g, ms):
                for m in ms:
                    to = acc1[:, m // 2, m % 2 * N:m % 2 * N + N]
                    for i, w in enumerate((w0_lo, w0_hi)):
                        last = nc.tensor.matmul(to, w[:, m * P:(m + 1) * P], x_hi[:, 0, 0:N],
                                                start=m % 2 == 0 and i == 0, stop=False, skip_group_check=True)
                return last

            def transpose_chunk(g, c):
                j = c + 1
                pe.wait_ge(s_chunk[c], LANDED * (g + 1))
                for i in range(GT):
                    last = nc.tensor.transpose(tp[:, j % 2, i * P:(i + 1) * P], emb[:, c, i, EMB],
                                               ident[:, :])
                last.then_inc(s_t, 1)

            def chunk_product(g, c, first=False):
                j = c + 1
                if first:
                    pe.wait_ge(s_wlo, c + 2)
                pe.wait_ge(s_xlo, STEPS * g + j + 1)
                for m in range(M1):
                    if m == 1 and c + 1 < CHUNKS:
                        transpose_chunk(g, c + 1)
                    last = product(acc1[:, m // 2, :], m, w1_hi, w1_lo, c, x_hi[:, j % 2, 0:N],
                                   x_lo[:, j % 2, 0:N], False, c == CHUNKS - 1)
                    if c == CHUNKS - 1 and m % 2 == 1:
                        last.then_inc(s_l1, 1)
                if c < CHUNKS - 1:
                    last.then_inc(s_xused, 1)

            def layer2(g):
                for k0, k1, m0, m1 in ([(k, k + 1, 0, M2) for k in range(M1 - 2)]
                                       + [(M1 - 2, M1, m, m + 2) for m in range(0, M2, 2)]):
                    for k in range(k0, k1):
                        b = k // 2
                        if k % 2 == 0 and m0 == 0:
                            pe.wait_ge(s_h1lo, M1 // 2 * g + b + 1)
                        x = slice(k % 2 * N, k % 2 * N + N)
                        for m in range(m0, m1):
                            last = product(acc2[:, m // 2, :], m, w2_hi, w2_lo, k, h1_hi[:, b % 2, x],
                                           h1_lo[:, b % 2, x], k == 0, k == M1 - 1)
                    if k0 == M1 - 2:
                        last.then_inc(s_l2, 1)
                    elif k0 % 2 == 1:
                        last.then_inc(s_h1used, 1)

            def layer3(g):
                for k in range(M2):
                    b = k // 2
                    if k % 2 == 0:
                        pe.wait_ge(s_h2lo, M2 // 2 * g + b + 1)
                    x = slice(k % 2 * N, k % 2 * N + N)
                    for m in range(M3):
                        last = product(acc1[:, 0, :], m, w3_hi, w3_lo, k, h2_hi[:, b, x], h2_lo[:, b, x],
                                       k == 0, k == M2 - 1)
                last.then_inc(s_l3, 1)

            def layer4(g):
                for i in range(GT):
                    for k in range(M3):
                        last = nc.tensor.matmul(acc2[:, 0, i:i + 1], h3[:, k * N + i * P:k * N + (i + 1) * P],
                                                wo[:, k:k + 1], start=(k == 0), stop=(k == M3 - 1))
                last.then_inc(s_l4, 1)

            def group(g, last):
                dense_load(g)
                transpose_chunk(g, 0)
                layer2(last)
                layer3(last)
                pe.wait_ge(s_xlo, STEPS * g + 1)
                dense_product(g, range(2, M1))
                pe.wait_ge(s_h3, last + 1)
                dense_product(g, range(0, 2)).then_inc(s_xused, 1)
                layer4(last)
                for c in range(CHUNKS):
                    chunk_product(g, c)

            pe.wait_ge(s_const, 32)
            pe.wait_ge(s_ident, 2)
            dense_load(0)
            transpose_chunk(0, 0)
            pe.wait_ge(s_wlo, 1)
            pe.wait_ge(s_xlo, 1)
            dense_product(0, range(M1)).then_inc(s_xused, 1)
            for c in range(CHUNKS):
                chunk_product(0, c, True)
            pe.wait_ge(s_wlo, UNITS)
            with pe.Fori(1, GROUPS) as g:
                group(g, g - 1)
            layer2(GROUPS - 1)
            layer3(GROUPS - 1)
            pe.wait_ge(s_h3, GROUPS)
            layer4(GROUPS - 1)


def kernel(**inputs):
    import numpy as np
    import concourse.bacc as bacc
    from concourse.bass_utils import run_bass_kernel_spmd as run

    a = {k: np.asarray(v) for k, v in inputs.items()}
    emb, lin = a["L0_rec_emb_tables"], a["L0_rec_lin_tables"]
    table = np.empty((FEATURES, VOCAB, ROW), np.float32)
    table[0::2, :, 0], table[0::2, :, 1:] = lin[0::2], emb[0::2]
    table[1::2, :, :DIM], table[1::2, :, DIM] = emb[1::2], lin[1::2]
    table = table.reshape(-1, ROW)
    ones = np.ones((BATCH, 2), np.float32)
    x = np.concatenate([a["r_dense"], ones], axis=1).reshape(P, GROUPS, GT, AUG)
    dense_t = np.ascontiguousarray(x.transpose(1, 3, 2, 0)).reshape(GROUPS, AUG, N)
    dense_w = np.zeros((AUG, 2 * DIM + 1), np.float32)
    dense_w[:13, 0:DIM] = a["L0_rec_Wd"]
    dense_w[:13, DIM:2 * DIM] = a["L0_rec_Wd"]
    dense_w[:13, 2 * DIM:] = a["L0_rec_Wld"]
    dense_w[13, 2 * DIM] = a["L0_rec_bld"][0]
    dense_w[14, 2 * DIM] = a["L0_rec_bias"][0, 0]
    w_out = np.ascontiguousarray(a["L0_rec_Wout"].reshape(M3, P).T)
    arrays = {"table": table, "idx": a["r_sparse_idx"], "dense_t": dense_t, "dense_w": dense_w,
              "w1": a["L0_rec_W1"], "w2": a["L0_rec_W2"], "w3": a["L0_rec_W3"], "w_out": w_out}
    arrays = {k: np.ascontiguousarray(v) for k, v in arrays.items()}

    nc = bacc.Bacc("TRN2", target_bir_lowering=False, num_devices=1)
    args = [nc.dram_tensor(k, v.shape, mybir.dt.from_np(v.dtype), kind="ExternalInput").ap() for k, v in arrays.items()]
    out = nc.dram_tensor("y_out", (BATCH, 1), F32, kind="ExternalOutput").ap()
    deepfm(nc, *args, out)
    return run(nc, [arrays], core_ids=[0]).results[0]["y_out"]
```
